# Optimizing a Trainium2 kernel written in Bass

```python
import numpy as np
import jax
import jax.numpy as jnp

def _softmax(x, axis=-1):
    return jax.nn.softmax(x, axis=axis)

def _gelu(x):
    return jax.nn.gelu(x, approximate=True)

def _silu(x):
    return jax.nn.silu(x)

def _sigmoid(x):
    return jax.nn.sigmoid(x)

def _layernorm(x, axis=-1, eps=1e-05):
    m = jnp.mean(x, axis=axis, keepdims=True)
    v = jnp.var(x, axis=axis, keepdims=True)
    return (x - m) / jnp.sqrt(v + eps)

def _scatter_add(tgt, idx, src, axis=0):
    return tgt.at[idx].add(src)

def _segment_sum(src, seg, n):
    return jax.ops.segment_sum(src, seg, n)
kernel_name = 'mk_recurrent_d1_jaxref_r8_c43bff'

def setup_inputs(seed: int=0):
    np.random.seed(seed)
    _w = jnp.asarray

    def _L0_attn_setup():
        import jax, jax.numpy as jnp
        import numpy as np
        HIDDEN = 512
        HEAD_DIM = 128
        N_Q_HEADS = 32
        N_KV_HEADS = 8
        SLIDING_WINDOW = 128
        ROPE_THETA = 10000.0
        BATCH, SEQ = (1, 256)

        def _rope(t, pos):
            d = t.shape[-1]
            half = d // 2
            inv_freq = ROPE_THETA ** (-jnp.arange(half, dtype=jnp.float32) / half)
            ang = pos[:, None].astype(jnp.float32) * inv_freq[None, :]
            cos = jnp.cos(ang)[None, :, None, :]
            sin = jnp.sin(ang)[None, :, None, :]
            t1, t2 = (t[..., :half], t[..., half:])
            return jnp.concatenate([t1 * cos - t2 * sin, t1 * sin + t2 * cos], axis=-1)
        key = jax.random.key(seed)
        ks = jax.random.split(key, 5)
        w_scale = HIDDEN ** (-0.5)
        return {'x': jax.random.normal(ks[0], (BATCH, SEQ, HIDDEN), jnp.float32), 'wq': jax.random.normal(ks[1], (HIDDEN, N_Q_HEADS * HEAD_DIM), jnp.float32) * w_scale, 'wk': jax.random.normal(ks[2], (HIDDEN, N_KV_HEADS * HEAD_DIM), jnp.float32) * w_scale, 'wv': jax.random.normal(ks[3], (HIDDEN, N_KV_HEADS * HEAD_DIM), jnp.float32) * w_scale, 'wo': jax.random.normal(ks[4], (N_Q_HEADS * HEAD_DIM, HIDDEN), jnp.float32) * w_scale}
    _L0_attn_in = _L0_attn_setup()

    def _L0_ffn_setup():
        import jax, jax.numpy as jnp
        import numpy as np
        GROUP_SIZE = 128

        def dequantize(imatrix, scales, zeros, group_size, out_dtype):
            rs = jnp.repeat(scales, group_size, axis=0)
            rz = jnp.repeat(zeros, group_size, axis=0)
            return ((imatrix.astype(rs.dtype) - rz.astype(rs.dtype)) * rs).astype(out_dtype)
        key = jax.random.key(seed)
        ks = jax.random.split(key, 10)
        H, I, G = (512, 1792, GROUP_SIZE)
        B, S = (4, 256)
        x = jax.random.normal(ks[0], (B, S, H), dtype=jnp.float32)
        gate_w = jax.random.randint(ks[1], (H, I), 0, 16, dtype=jnp.int32)
        gate_z = jax.random.randint(ks[2], (H // G, I), 0, 16, dtype=jnp.int32)
        gate_s = jax.random.uniform(ks[3], (H // G, I), dtype=jnp.float32) * 0.01
        up_w = jax.random.randint(ks[4], (H, I), 0, 16, dtype=jnp.int32)
        up_z = jax.random.randint(ks[5], (H // G, I), 0, 16, dtype=jnp.int32)
        up_s = jax.random.uniform(ks[6], (H // G, I), dtype=jnp.float32) * 0.01
        down_w = jax.random.randint(ks[7], (I, H), 0, 16, dtype=jnp.int32)
        down_z = jax.random.randint(ks[8], (I // G, H), 0, 16, dtype=jnp.int32)
        down_s = jax.random.uniform(ks[9], (I // G, H), dtype=jnp.float32) * 0.01
        return {'x': x, 'gate_w': gate_w, 'gate_z': gate_z, 'gate_s': gate_s, 'up_w': up_w, 'up_z': up_z, 'up_s': up_s, 'down_w': down_w, 'down_z': down_z, 'down_s': down_s}
    _L0_ffn_in = _L0_ffn_setup()
    _d = {'L0_attn_x': _L0_attn_in['x'], 'L0_attn_wq': _L0_attn_in['wq'], 'L0_attn_wk': _L0_attn_in['wk'], 'L0_attn_wv': _L0_attn_in['wv'], 'L0_attn_wo': _L0_attn_in['wo'], 'L0_ffn_gate_w': _L0_ffn_in['gate_w'], 'L0_ffn_gate_z': _L0_ffn_in['gate_z'], 'L0_ffn_gate_s': _L0_ffn_in['gate_s'], 'L0_ffn_up_w': _L0_ffn_in['up_w'], 'L0_ffn_up_z': _L0_ffn_in['up_z'], 'L0_ffn_up_s': _L0_ffn_in['up_s'], 'L0_ffn_down_w': _L0_ffn_in['down_w'], 'L0_ffn_down_z': _L0_ffn_in['down_z'], 'L0_ffn_down_s': _L0_ffn_in['down_s']}
    _x0 = _d['L0_attn_x']
    _d['L0_attn_x'] = jax.random.normal(jax.random.fold_in(jax.random.key(seed), 1), (2, 512, 512), dtype=_x0.dtype)
    del _x0
    return _d

def reference(L0_attn_x, L0_attn_wq, L0_attn_wk, L0_attn_wv, L0_attn_wo, L0_ffn_gate_w, L0_ffn_gate_z, L0_ffn_gate_s, L0_ffn_up_w, L0_ffn_up_z, L0_ffn_up_s, L0_ffn_down_w, L0_ffn_down_z, L0_ffn_down_s):

    def _L0_attn_ref(x, wq, wk, wv, wo):
        import jax, jax.numpy as jnp
        import numpy as np
        HIDDEN = 512
        HEAD_DIM = 128
        N_Q_HEADS = 32
        N_KV_HEADS = 8
        SLIDING_WINDOW = 128
        ROPE_THETA = 10000.0
        BATCH, SEQ = (1, 256)

        def _rope(t, pos):
            d = t.shape[-1]
            half = d // 2
            inv_freq = ROPE_THETA ** (-jnp.arange(half, dtype=jnp.float32) / half)
            ang = pos[:, None].astype(jnp.float32) * inv_freq[None, :]
            cos = jnp.cos(ang)[None, :, None, :]
            sin = jnp.sin(ang)[None, :, None, :]
            t1, t2 = (t[..., :half], t[..., half:])
            return jnp.concatenate([t1 * cos - t2 * sin, t1 * sin + t2 * cos], axis=-1)
        B, S, _ = x.shape
        G = N_Q_HEADS // N_KV_HEADS
        sm_scale = HEAD_DIM ** (-0.5)
        q = (x @ wq).reshape(B, S, N_Q_HEADS, HEAD_DIM)
        k = (x @ wk).reshape(B, S, N_KV_HEADS, HEAD_DIM)
        v = (x @ wv).reshape(B, S, N_KV_HEADS, HEAD_DIM)
        pos = jnp.arange(S)
        q = _rope(q, pos)
        k = _rope(k, pos)
        qg = q.reshape(B, S, N_KV_HEADS, G, HEAD_DIM)
        scores = jnp.einsum('bqhgd,bshd->bhgqs', qg, k) * sm_scale
        i = pos[:, None]
        j = pos[None, :]
        allowed = (j <= i) & (j > i - SLIDING_WINDOW)
        neg = jnp.finfo(scores.dtype).min
        scores = jnp.where(allowed[None, None, None], scores, neg)
        attn = jax.nn.softmax(scores, axis=-1)
        out = jnp.einsum('bhgqs,bshd->bqhgd', attn, v).reshape(B, S, N_Q_HEADS * HEAD_DIM)
        return out @ wo

    def _L0_ffn_ref(x, gate_w, gate_z, gate_s, up_w, up_z, up_s, down_w, down_z, down_s):
        import jax, jax.numpy as jnp
        import numpy as np
        GROUP_SIZE = 128

        def dequantize(imatrix, scales, zeros, group_size, out_dtype):
            rs = jnp.repeat(scales, group_size, axis=0)
            rz = jnp.repeat(zeros, group_size, axis=0)
            return ((imatrix.astype(rs.dtype) - rz.astype(rs.dtype)) * rs).astype(out_dtype)
        dt = x.dtype
        gate_proj = dequantize(gate_w, gate_s, gate_z, GROUP_SIZE, dt)
        up_proj = dequantize(up_w, up_s, up_z, GROUP_SIZE, dt)
        down_proj = dequantize(down_w, down_s, down_z, GROUP_SIZE, dt)
        gate = jax.nn.silu(jnp.dot(x, gate_proj))
        up = jnp.dot(x, up_proj)
        return jnp.dot(gate * up, down_proj)
    x = L0_attn_x
    xn = _layernorm(x, axis=-1)
    s = _L0_attn_ref(xn, L0_attn_wq, L0_attn_wk, L0_attn_wv, L0_attn_wo)
    g = _silu(_L0_ffn_ref(xn, L0_ffn_gate_w, L0_ffn_gate_z, L0_ffn_gate_s, L0_ffn_up_w, L0_ffn_up_z, L0_ffn_up_s, L0_ffn_down_w, L0_ffn_down_z, L0_ffn_down_s))
    x = x + s * g
    return x

_drawn_inputs = setup_inputs


def setup_inputs(seed=0):
    import zlib

    import numpy as np

    out = dict(_drawn_inputs(seed))
    spreads = {}
    factors = {}
    for name, (base, spread) in spreads.items():
        noise = np.random.default_rng([zlib.crc32(name.encode()), seed]).standard_normal(out[name].shape)
        drawn = base * np.exp(spread * noise) if base else spread * noise
        out[name] = jnp.asarray(drawn.astype(out[name].dtype))
    for name, factor in factors.items():
        out[name] = (out[name] * factor).astype(out[name].dtype)
    return out
```

```python
from contextlib import ExitStack

import numpy as np
import concourse.bass as bass
from concourse import mybir

F32 = mybir.dt.float32
F32R = mybir.dt.float32r
I32 = mybir.dt.int32
ALU = mybir.AluOpType
ACT = mybir.ActivationFunctionType

P = 128
BATCH, SEQ, HID = 2, 512, 512
TOK = BATCH * SEQ
KT = HID // P
TT = TOK // P
QB = SEQ // P
NKV, GQ = 8, 4
INTER = 1792
NI = INTER // P
PAIRS = NI // 2
EPS = 1e-5
SM_SCALE = float(P) ** -0.5
MASKED = -3.0e38


def wait(eng, sem, count):
    if isinstance(count, int) and count <= 0:
        return
    eng.wait_ge(sem, count)


def three_passes(pe, out, stat, mov, first, last):
    pe.matmul(out, stat[1], mov[0], start=first, stop=False)
    pe.matmul(out, stat[0], mov[1], start=False, stop=False)
    return pe.matmul(out, stat[0], mov[0], start=False, stop=last)


def norm_phase(nc, x, ident_in, ident, xt_hi, xt_lo):
    with ExitStack() as ctx:
        sb = lambda name, shape, dt=F32: ctx.enter_context(nc.sbuf_tensor(name, shape, dt))
        sem = lambda name: ctx.enter_context(nc.semaphore(name))
        xin = sb("xin", [P, TT, HID])
        xn = sb("xn", [P, TT, HID])
        stats = sb("stats", [P, TT, 6])
        mv = sb("mv", [P, TT, 2])
        var = sb("var", [P, TT])
        root = sb("root", [P, TT])
        r0 = sb("r0", [P, TT])
        r2 = sb("r2", [P, TT])
        corr = sb("corr", [P, TT])
        rstd = sb("rstd", [P, TT])
        ps = ctx.enter_context(nc.psum_tensor("norm_ps", [P, 8, HID], F32))
        x_in = [sem(f"x_in{t}") for t in range(TT)]
        id_in = sem("id_in")
        stat_done = sem("stat_done")
        var_done = sem("var_done")
        root_done = sem("root_done")
        newton = sem("newton")
        xn_done = sem("xn_done")
        turned = sem("turned")
        hi_done = sem("hi_done")
        lo_done = sem("lo_done")
        block = ctx.enter_context(nc.Block())

        @block.sync
        def _(sp):
            for t in range(0, TT, 2):
                sp.dma_start(xin[:, t, :], x[t * P:(t + 1) * P, :]).then_inc(x_in[t], 16)
            sp.dma_start(ident[:, :], ident_in).then_inc(id_in, 16)

        @block.vector
        def _(dve):
            for t in range(TT):
                dve.wait_ge(x_in[t], 16)
                dve.bn_stats(stats[:, t, :], xin[:, t, :]).then_inc(stat_done, 1)
                dve.wait_ge(stat_done, t + 1)
                dve.bn_aggr(mv[:, t, :], stats[:, t, :]).then_inc(var_done, 1)
            dve.wait_ge(var_done, TT)
            dve.tensor_scalar(var[:, :], mv[:, :, 1], EPS, None, ALU.add).then_inc(var_done, 1)
            dve.wait_ge(root_done, 1)
            dve.reciprocal(r0[:, :], root[:, :]).then_inc(newton, 1)
            dve.wait_ge(newton, 1)
            dve.tensor_tensor(r2[:, :], r0[:, :], r0[:, :], ALU.mult).then_inc(newton, 1)
            dve.wait_ge(newton, 2)
            dve.tensor_tensor(corr[:, :], r2[:, :], var[:, :], ALU.mult).then_inc(newton, 1)
            dve.wait_ge(newton, 3)
            dve.tensor_scalar(r2[:, :], corr[:, :], -0.5, 1.5, ALU.mult, ALU.add).then_inc(newton, 1)
            dve.wait_ge(newton, 4)
            dve.tensor_tensor(rstd[:, :], r0[:, :], r2[:, :], ALU.mult).then_inc(newton, 1)
            dve.wait_ge(newton, 5)
            for t in range(TT):
                dve.tensor_scalar(xn[:, t, :], xin[:, t, :], mv[:, t, 0:1], rstd[:, t:t + 1],
                                  ALU.subtract, ALU.mult).then_inc(xn_done, 1)
            for t in range(TT):
                dve.wait_ge(hi_done, t + 1)
                out = xt_lo[:, :, t * P:(t + 1) * P]
                dve.tensor_tensor(out, ps[:, t, :].rearrange("p (k c) -> p k c", k=KT),
                                  xt_hi[:, :, t * P:(t + 1) * P].bitcast(F32), ALU.subtract).then_inc(lo_done, 1)

        @block.scalar
        def _(act):
            for t in range(1, TT, 2):
                act.dma_start(xin[:, t, :], x[t * P:(t + 1) * P, :]).then_inc(x_in[t], 16)
            act.wait_ge(var_done, TT + 1)
            act.activation(root[:, :], var[:, :], ACT.Sqrt).then_inc(root_done, 1)
            for t in range(TT):
                act.wait_ge(turned, t + 1)
                act.activation(xt_hi[:, :, t * P:(t + 1) * P],
                               ps[:, t, :].rearrange("p (k c) -> p k c", k=KT), ACT.Copy).then_inc(hi_done, 1)

        @block.tensor
        def _(pe):
            pe.wait_ge(id_in, 16)
            for t in range(TT):
                pe.wait_ge(xn_done, t + 1)
                for k in range(KT):
                    last = pe.transpose(ps[:, t, k * P:(k + 1) * P], xn[:, t, k * P:(k + 1) * P], ident[:, :])
                last.then_inc(turned, 1)


def ffn_phase(nc, weights, xt_hi, xt_lo, gate_dram):
    gate_w, gate_z, gate_s, up_w, up_z, up_s, down_w, down_z, down_s = weights
    HALVES = TOK // 512
    with ExitStack() as ctx:
        sb = lambda name, shape, dt=F32: ctx.enter_context(nc.sbuf_tensor(name, shape, dt))
        sem = lambda name: ctx.enter_context(nc.semaphore(name))
        RING, DQ = 3, 2
        raw_w = [sb(f"raw_w{s}", [P, KT, P], I32) for s in range(RING)]
        raw_z = [sb(f"raw_z{s}", [P, KT, P], I32) for s in range(RING)]
        raw_s = [sb(f"raw_s{s}", [P, KT, P]) for s in range(RING)]
        dq = [sb(f"dq{s}", [P, KT, P]) for s in range(DQ)]
        w_hi = sb("fw_hi", [P, 6, KT, P], F32R)
        w_lo = sb("fw_lo", [P, 6, KT, P], F32R)
        sil = sb("sil", [P, 2, 512])
        mid = sb("mid", [P, 2, 512])
        mid_hi = sb("mid_hi", [P, 2, TOK], F32R)
        mid_lo = sb("mid_lo", [P, 2, TOK], F32R)
        acc = sb("ffn_acc", [P, TT, HID])
        ps = ctx.enter_context(nc.psum_tensor("ffn_ps", [P, 8, 512], F32))
        ps_gate, ps_up, ps_down = ps[:, 0:2, :], ps[:, 2:4, :], ps[:, 4:8, :]
        raw_in = [sem(f"raw_in{s}") for s in range(RING)]
        zero_off = sem("zero_off")
        scaled = sem("scaled")
        w_hi_done = sem("fw_hi_done")
        w_split = sem("fw_split")
        gu_ready = sem("gu_ready")
        silu_done = sem("silu_done")
        mid_done = sem("mid_done")
        mid_hi_done = sem("mid_hi_done")
        mid_split = sem("mid_split")
        down_ready = sem("down_ready")
        acc_done = sem("acc_done")
        gate_done = sem("gate_done")
        gate_out = sem("gate_out")
        block = ctx.enter_context(nc.Block())

        GATE, UP, DOWN = 0, 1, 2
        AHEAD = [(GATE, 0), (UP, 0), (GATE, 1), (UP, 1)]
        IN_BODY = [(DOWN, 0), (DOWN, 1)] + AHEAD
        slot_of = lambda kind, ii: 4 + ii if kind == DOWN else 2 * ii + kind

        def piece_index(n, at):
            return n * 6 + (4 + at)

        def ring_slot(at):
            return (4 + at) % RING

        def rounds(n, at):
            return n * 2 + (4 + at) // RING

        def load_piece(eng, n, at, kind, ii, pair):
            s = ring_slot(at)
            wait(eng, w_split, piece_index(n, at) - RING + 1)
            cols = bass.ds(pair * (2 * P) + ii * P, P)
            if kind == DOWN:
                flat = lambda t: t[:, :, :].rearrange("p k c -> p (k c)")
                row = bass.ds(pair * 2 + ii, 1)
                eng.dma_start(flat(raw_w[s]), down_w[cols, :]).then_inc(raw_in[s], 16)
                eng.dma_start(flat(raw_z[s]), down_z[row, :].rearrange("a c -> (a c)").partition_broadcast(P)).then_inc(raw_in[s], 16)
                eng.dma_start(flat(raw_s[s]), down_s[row, :].rearrange("a c -> (a c)").partition_broadcast(P)).then_inc(raw_in[s], 16)
            else:
                w, z, sc = (gate_w, gate_z, gate_s) if kind == GATE else (up_w, up_z, up_s)
                eng.dma_start(raw_w[s][:, :, :], w[:, cols].rearrange("(k p) c -> p k c", p=P)).then_inc(raw_in[s], 16)
                eng.dma_start(raw_z[s][:, :, :], z[:, cols].partition_broadcast(P)).then_inc(raw_in[s], 16)
                eng.dma_start(raw_s[s][:, :, :], sc[:, cols].partition_broadcast(P)).then_inc(raw_in[s], 16)

        def dequantise(dve, n, at):
            s, q = ring_slot(at), at % DQ
            k = piece_index(n, at)
            dve.wait_ge(raw_in[s], (rounds(n, at) + 1) * 48)
            wait(dve, w_split, k - DQ + 1)
            dve.tensor_tensor(dq[q][:, :, :], raw_w[s][:, :, :], raw_z[s][:, :, :], ALU.subtract).then_inc(zero_off, 1)
            dve.wait_ge(zero_off, k + 1)
            dve.tensor_tensor(dq[q][:, :, :], dq[q][:, :, :], raw_s[s][:, :, :], ALU.mult).then_inc(scaled, 1)

        def weight_hi(act, n, at, kind, ii):
            act.wait_ge(scaled, piece_index(n, at) + 1)
            act.activation(w_hi[:, slot_of(kind, ii), :, :], dq[at % DQ][:, :, :], ACT.Copy).then_inc(w_hi_done, 1)

        def weight_lo(pool, n, at, kind, ii):
            pool.wait_ge(w_hi_done, piece_index(n, at) + 1)
            to = slot_of(kind, ii)
            pool.tensor_tensor(w_lo[:, to, :, :], dq[at % DQ][:, :, :], w_hi[:, to, :, :].bitcast(F32),
                               ALU.subtract).then_inc(w_split, 1)

        def pieces(at0, at1):
            return [(at, *IN_BODY[at]) for at in range(at0, at1)]

        def over_pairs(eng, body):
            body(0, False)
            with eng.Fori(1, PAIRS - 1) as n:
                body(n, False)
            body(PAIRS - 1, True)

        @block.sync
        def _(sp):
            for at, (kind, ii) in enumerate(AHEAD):
                load_piece(sp, 0, at - 4, kind, ii, 0)

            def body(n, last):
                for at, kind, ii in pieces(0, 2 if last else 6):
                    load_piece(sp, n, at, kind, ii, n if at < 2 else n + 1)
            over_pairs(sp, body)
            for t in range(TT):
                sp.wait_ge(gate_done, t + 1)
                sp.dma_start(gate_dram[t * P:(t + 1) * P, :], acc[:, t, :]).then_inc(gate_out, 16)
            sp.wait_ge(gate_out, 16 * TT)

        @block.tensor
        def _(pe):
            def gate_up(n, ii, hf):
                e = n * 4 + (2 * ii + hf)
                for kind, bank in ((GATE, ps_gate), (UP, ps_up)):
                    wait(pe, w_split, piece_index(n, 0) - 4 + (2 * ii + kind) + 1)
                    if kind == GATE:
                        wait(pe, silu_done, e - 1)
                    else:
                        wait(pe, mid_done, e - 1)
                    s = slot_of(kind, ii)
                    for k in range(KT):
                        last = three_passes(pe, bank[:, hf, :], (w_hi[:, s, k, :], w_lo[:, s, k, :]),
                                            (xt_hi[:, k, hf * 512:(hf + 1) * 512], xt_lo[:, k, hf * 512:(hf + 1) * 512]),
                                            k == 0, k == KT - 1)
                    last.then_inc(gu_ready, 1)

            def down(n, t):
                pe.wait_ge(mid_split, n * 4 + (3 if t < TT // 2 else 4))
                wait(pe, w_split, piece_index(n, 0) + 2)
                wait(pe, acc_done, n * TT + (t - 4 + 1))
                for ii in range(2):
                    s = slot_of(DOWN, ii)
                    flat = lambda w: w[:, s, :, :].rearrange("p k c -> p (k c)")
                    last = three_passes(pe, ps_down[:, t % 4, :],
                                        (mid_hi[:, ii, t * P:(t + 1) * P], mid_lo[:, ii, t * P:(t + 1) * P]),
                                        (flat(w_hi), flat(w_lo)), ii == 0, ii == 1)
                last.then_inc(down_ready, 1)

            def body(n, last):
                for ii in range(2):
                    for hf in range(HALVES):
                        gate_up(n, ii, hf)
                for t in range(TT):
                    down(n, t)
            over_pairs(pe, body)

        @block.scalar
        def _(act):
            for at, (kind, ii) in enumerate(AHEAD):
                weight_hi(act, 0, at - 4, kind, ii)

            def silu(n, ii, hf):
                e = n * 4 + (2 * ii + hf)
                act.wait_ge(gu_ready, e * 2 + 1)
                wait(act, mid_done, e - 1)
                act.activation(sil[:, hf, :], ps_gate[:, hf, :], ACT.Silu).then_inc(silu_done, 1)
                act.wait_ge(mid_done, e + 1)
                act.activation(mid_hi[:, ii, hf * 512:(hf + 1) * 512], mid[:, hf, :], ACT.Copy).then_inc(mid_hi_done, 1)

            def body(n, last):
                wait(act, down_ready, n * TT)
                for at, kind, ii in pieces(0, 2):
                    weight_hi(act, n, at, kind, ii)
                for i in range(2):
                    silu(n, i, 0)
                    silu(n, i, 1)
                    if not last:
                        for at, kind, ii in pieces(2 + 2 * i, 4 + 2 * i):
                            weight_hi(act, n, at, kind, ii)
            over_pairs(act, body)
            for t in range(TT):
                act.wait_ge(acc_done, TT * (PAIRS - 1) + t + 1)
                act.activation(acc[:, t, :], acc[:, t, :], ACT.Silu).then_inc(gate_done, 1)

        @block.gpsimd
        def _(pool):
            for at, (kind, ii) in enumerate(AHEAD):
                weight_lo(pool, 0, at - 4, kind, ii)

            def split_mid(n, ii, hf):
                e = n * 4 + (2 * ii + hf)
                pool.wait_ge(mid_hi_done, e + 1)
                cols = slice(hf * 512, (hf + 1) * 512)
                pool.tensor_tensor(mid_lo[:, ii, cols], mid[:, hf, :], mid_hi[:, ii, cols].bitcast(F32),
                                   ALU.subtract).then_inc(mid_split, 1)

            def body(n, last):
                for at, kind, ii in pieces(0, 2):
                    weight_lo(pool, n, at, kind, ii)
                for i in range(2):
                    split_mid(n, i, 0)
                    split_mid(n, i, 1)
                    if not last:
                        for at, kind, ii in pieces(2 + 2 * i, 4 + 2 * i):
                            weight_lo(pool, n, at, kind, ii)
            over_pairs(pool, body)

        @block.vector
        def _(dve):
            for at in range(4):
                dequantise(dve, 0, at - 4)

            def middle(n, ii, hf):
                e = n * 4 + (2 * ii + hf)
                dve.wait_ge(gu_ready, e * 2 + 2)
                dve.wait_ge(silu_done, e + 1)
                wait(dve, mid_split, e - 1)
                dve.tensor_tensor(mid[:, hf, :], sil[:, hf, :], ps_up[:, hf, :], ALU.mult).then_inc(mid_done, 1)

            def body(n, last):
                for at in range(2):
                    dequantise(dve, n, at)
                for i in range(2):
                    middle(n, i, 0)
                    middle(n, i, 1)
                    if not last:
                        for at in range(2 + 2 * i, 4 + 2 * i):
                            dequantise(dve, n, at)
                for t in range(TT):
                    dve.wait_ge(down_ready, n * TT + (t + 1))
                    if isinstance(n, int) and n == 0:
                        dve.tensor_copy(acc[:, t, :], ps_down[:, t % 4, :]).then_inc(acc_done, 1)
                    else:
                        dve.tensor_tensor(acc[:, t, :], ps_down[:, t % 4, :], acc[:, t, :], ALU.add).then_inc(acc_done, 1)
            over_pairs(dve, body)


def attention_phase(nc, wq, wk, wv, wo, cos_in, sin_in, mask_in, ident, xt_hi, xt_lo, y):
    V_, K_, Q_, WO_ = 0, 1, 2, 6
    NPIECE = 10
    RING = 5
    PROJ = 7
    with ExitStack() as ctx:
        sb = lambda name, shape, dt=F32: ctx.enter_context(nc.sbuf_tensor(name, shape, dt))
        sem = lambda name: ctx.enter_context(nc.semaphore(name))
        cos = sb("cos", [P, SEQ])
        sin = sb("sin", [P, SEQ])
        mask = sb("mask_sb", [P, 2 * P])
        raw = [sb(f"raw{s}", [P, 512]) for s in range(RING)]
        w_hi = sb("w_hi", [P, 6, KT, P], F32R)
        w_lo = sb("w_lo", [P, 6, KT, P], F32R)
        wo_hi = sb("wo_hi", [P, 2 * GQ * HID], F32R)
        wo_lo = sb("wo_lo", [P, 2 * GQ * HID], F32R)
        q_hi = sb("q_hi", [P, 2, GQ, SEQ], F32R)
        q_lo = sb("q_lo", [P, 2, GQ, SEQ], F32R)
        k_hi = sb("k_hi", [P, 2, P + SEQ], F32R)
        k_lo = sb("k_lo", [P, 2, P + SEQ], F32R)
        v_t = sb("v_t", [P, SEQ])
        v_hi = sb("v_hi", [P, 2, QB, P], F32R)
        v_lo = sb("v_lo", [P, 2, QB, P], F32R)
        swap = sb("swap", [P, 2, SEQ])
        direct = sb("direct", [P, 2, SEQ])
        roped = sb("roped", [P, 2, SEQ])
        probs = sb("probs", [P, GQ, 2 * P])
        neg_max = sb("neg_max", [P, GQ])
        total = sb("total", [P, GQ])
        waited = sb("waited", [P, 2])
        inv = sb("inv", [P, GQ])
        pt_hi = sb("pt_hi", [P, 2, GQ * P], F32R)
        pt_lo = sb("pt_lo", [P, 2, GQ * P], F32R)
        o_hi = sb("o_hi", [P, GQ, P], F32R)
        o_lo = sb("o_lo", [P, GQ, P], F32R)
        ps = ctx.enter_context(nc.psum_tensor("att_ps", [P, 8, 512], F32))
        ps_proj = ps[:, 0:2, :]
        ps_score = ps[:, 2:4, :].rearrange("p a (h c) -> p (a h) c", h=2)
        ps_pt = ps[:, 4:6, :]
        ps_o = ps[:, 6, :]
        ps_y = ps[:, 7, :]

        table_in = sem("table_in")
        pad_done = sem("pad_done")
        raw_in = [sem(f"att_raw_in{s}") for s in range(RING)]
        w_hi_done = sem("w_hi_done")
        w_split = sem("w_split")
        proj_ready = sem("proj_ready")
        proj_drained = sem("proj_drained")
        v_hi_done = sem("v_hi_done")
        swapped = sem("swapped")
        sin_part = sem("sin_part")
        rope_sum = sem("rope_sum")
        rope_hi = sem("rope_hi")
        rope_split = sem("rope_split")
        scores_ready = sem("scores_ready")
        shifted = sem("shifted")
        bank_seen = sem("bank_seen")
        exp_done = sem("exp_done")
        inv_done = sem("inv_done")
        probs_ready = sem("probs_ready")
        pt_ready = sem("pt_ready")
        pt_hi_done = sem("pt_hi_done")
        pt_split = sem("pt_split")
        o_ready = sem("o_ready")
        o_hi_done = sem("o_hi_done")
        o_split = sem("o_split")
        y_ready = sem("y_ready")
        y_added = sem("y_added")
        block = ctx.enter_context(nc.Block())

        def over_heads(eng, body):
            body(0, False)
            with eng.Fori(1, NKV - 1) as g:
                body(g, False)
            body(NKV - 1, True)

        def load_weight(eng, g, p):
            s = p % RING
            wait(eng, w_split, g * NPIECE + (p - RING + 1))
            if p >= WO_:
                src = wo[bass.ds(g * (GQ * P) + (p - WO_) * P, P), :]
                dst = raw[s][:, :]
            else:
                w, col = ((wv, g * P), (wk, g * P))[p] if p < Q_ else (wq, g * (GQ * P) + (p - Q_) * P)
                src = w[:, bass.ds(col, P)].rearrange("(k p) c -> p k c", p=P)
                dst = raw[s][:, :].rearrange("p (k c) -> p k c", k=KT)
            eng.dma_start(dst, src).then_inc(raw_in[s], 16)

        def split_target(g, p):
            if p < WO_:
                flat = lambda w: w[:, p, :, :].rearrange("p k c -> p (k c)")
                return flat(w_hi), flat(w_lo)
            half = (g & 1) * (GQ * HID) if not isinstance(g, int) else (g % 2) * GQ * HID
            at = bass.ds(half + (p - WO_) * HID, HID)
            return wo_hi[:, at], wo_lo[:, at]

        def weight_hi(act, g, p):
            act.wait_ge(raw_in[p % RING], g * 32 + (p // RING + 1) * 16)
            act.activation(split_target(g, p)[0], raw[p % RING][:, :], ACT.Copy).then_inc(w_hi_done, 1)

        def weight_lo(pool, g, p):
            pool.wait_ge(w_hi_done, g * NPIECE + (p + 1))
            hi, lo = split_target(g, p)
            pool.tensor_tensor(lo, raw[p % RING][:, :], hi.bitcast(F32), ALU.subtract).then_inc(w_split, 1)

        SPLIT_AT = {(0, 1): (0, 1), (0, 2): (2, 3), (0, 3): (4,), (1, 0): (5, 6), (1, 1): (7,), (1, 2): (8,), (1, 3): (9,)}
        POSITION = {0: 0, 1: 1, 2: 3, 3: 4, 4: 5, 5: 6}

        @block.sync
        def _(sp):
            sp.dma_start(cos[:, :], cos_in).then_inc(table_in, 16)
            sp.dma_start(sin[:, :], sin_in).then_inc(table_in, 16)
            sp.dma_start(mask[:, :], mask_in).then_inc(table_in, 16)
            for p in range(NPIECE):
                load_weight(sp, 0, p)

            def body(g, last):
                if not last:
                    for p in range(NPIECE):
                        load_weight(sp, g + 1, p)
            over_heads(sp, body)

        @block.tensor
        def _(pe):
            def project(g, unit, b, k):
                if k == 2:
                    return turn_v(unit, b)
                p = k if k < 2 else k - 1
                wait(pe, w_split, g * NPIECE + (p + 1))
                wait(pe, proj_drained, unit * PROJ + (k - 1))
                for t in range(KT):
                    cols = slice(b * SEQ, (b + 1) * SEQ)
                    last = three_passes(pe, ps_proj[:, (PROJ * b + k) % 2, :], (w_hi[:, p, t, :], w_lo[:, p, t, :]),
                                        (xt_hi[:, t, cols], xt_lo[:, t, cols]), t == 0, t == KT - 1)
                last.then_inc(proj_ready, 1)

            def turn_v(unit, b):
                wait(pe, proj_drained, unit * PROJ + 1)
                for t in range(QB):
                    last = pe.transpose(ps_proj[:, (PROJ * b + 2) % 2, t * P:(t + 1) * P], v_t[:, t * P:(t + 1) * P], ident[:, :])
                last.then_inc(proj_ready, 1)

            def scores(n, unit, b, j):
                wait(pe, shifted, n * GQ)
                for h in range(GQ):
                    wait(pe, rope_split, unit * 5 + (h + 2))
                    q = [t[:, b, h, j * P:(j + 1) * P] for t in (q_hi, q_lo)]
                    k = [t[:, b, j * P:(j + 2) * P] for t in (k_hi, k_lo)]
                    last = three_passes(pe, ps_score[:, h, :], q, k, True, True)
                    if h % 2:
                        last.then_inc(scores_ready, 1)

            def turn_probs(n, j):
                wait(pe, pt_split, n)
                for h in range(GQ):
                    pe.wait_ge(probs_ready, n * GQ + (h + 1))
                    for w in range(0 if j else 1, 2):
                        last = pe.transpose(ps_pt[:, w, h * P:(h + 1) * P], probs[:, h, w * P:(w + 1) * P], ident[:, :])
                last.then_inc(pt_ready, 1)

            def weigh_values(n, unit, b, j):
                pe.wait_ge(pt_split, n + 1)
                pe.wait_ge(proj_drained, unit * PROJ + 3)
                wait(pe, o_split, n)
                windows = range(0 if j else 1, 2)
                for w in windows:
                    v = [t[:, b, j - 1 + w, :] for t in (v_hi, v_lo)]
                    last = three_passes(pe, ps_o[:, :], v, (pt_hi[:, w, :], pt_lo[:, w, :]), w == windows[0], w == 1)
                last.then_inc(o_ready, 1)

            def project_out(g, n):
                pe.wait_ge(o_split, n + 1)
                wait(pe, w_split, g * NPIECE + NPIECE)
                wait(pe, y_added, n)
                for h in range(GQ):
                    hi, lo = split_target(g, WO_ + h)
                    last = three_passes(pe, ps_y[:, :], (o_hi[:, h, :], o_lo[:, h, :]), (hi, lo), h == 0, h == GQ - 1)
                last.then_inc(y_ready, 1)

            pe.wait_ge(pad_done, 2)
            for k in range(PROJ):
                project(0, 0, 0, k)
            scores(0, 0, 0, 0)

            def body(g, last):
                for b in range(2):
                    unit = g * 2 + b
                    ahead = not (last and b == 1)
                    gn, un, bn = (g, g * 2 + 1, 1) if b == 0 else (g + 1, g * 2 + 2, 0)

                    def ahead_project(*ks):
                        if ahead:
                            for k in ks:
                                project(gn, un, bn, k)
                    for j in range(QB):
                        n = g * 8 + (4 * b + j)
                        if j == 0:
                            ahead_project(0)
                        turn_probs(n, j)
                        if j < QB - 1:
                            scores(g * 8 + (4 * b + j + 1), unit, b, j + 1)
                        ahead_project(*((1,), (2, 3), (5,), (6,))[j])
                        weigh_values(n, unit, b, j)
                        if j == 1:
                            ahead_project(4)
                        project_out(g, n)
                        if j == QB - 1 and ahead:
                            scores(g * 8 + (4 * b + j + 1), un, bn, 0)
            over_heads(pe, body)

        @block.scalar
        def _(act):
            def swap_halves(unit, b, i):
                k = 1 if i == 0 else i + 2
                par = (5 * b + i) % 2
                act.wait_ge(proj_ready, unit * PROJ + (k + 1))
                wait(act, rope_sum, unit * 5 + (i - 1))
                src = ps_proj[:, (PROJ * b + k) % 2, :]
                act.activation(swap[0:P // 2, par, :], src[P // 2:P, :], ACT.Copy)
                act.activation(swap[P // 2:P, par, :], src[0:P // 2, :], ACT.Copy).then_inc(swapped, 1)

            def rope_target(b, i):
                return (k_hi[:, b, P:P + SEQ], k_lo[:, b, P:P + SEQ]) if i == 0 else (q_hi[:, b, i - 1, :], q_lo[:, b, i - 1, :])

            def hi_of_roped(unit, b, i):
                act.wait_ge(rope_sum, unit * 5 + (i + 1))
                act.activation(rope_target(b, i)[0], roped[:, (5 * b + i) % 2, :], ACT.Copy).then_inc(rope_hi, 1)

            def hi_of_v(unit, b):
                act.wait_ge(proj_ready, unit * PROJ + 3)
                act.activation(v_hi[:, b, :, :], ps_proj[:, (PROJ * b + 2) % 2, :].rearrange("p (t c) -> p t c", t=QB),
                               ACT.Copy).then_inc(v_hi_done, 1)

            def exps(n, j):
                cols = slice(0 if j else P, 2 * P)
                for h in range(GQ):
                    act.wait_ge(shifted, n * GQ + (h + 1))
                    act.activation(probs[:, h, cols], probs[:, h, cols], ACT.Exp, scale=-1.0, bias=neg_max[:, h:h + 1],
                                   accum_out=total[:, h:h + 1]).then_inc(exp_done, 1)

            def hi_of_probs(n, j):
                act.wait_ge(pt_ready, n + 1)
                w = slice(0 if j else 1, 2)
                act.activation(pt_hi[:, w, :], ps_pt[:, w, :], ACT.Copy).then_inc(pt_hi_done, 1)

            def hi_of_o(n):
                act.wait_ge(o_ready, n + 1)
                act.activation(o_hi[:, :, :], ps_o.rearrange("p (h c) -> p h c", h=GQ), ACT.Copy).then_inc(o_hi_done, 1)

            for p in range(6):
                weight_hi(act, 0, p)
            swap_halves(0, 0, 0)
            hi_of_v(0, 0)
            hi_of_roped(0, 0, 0)
            for i in range(1, 5):
                swap_halves(0, 0, i)
                hi_of_roped(0, 0, i)
            for p in range(6, NPIECE):
                weight_hi(act, 0, p)
            exps(0, 0)

            def body(g, last):
                for b in range(2):
                    ahead = not (last and b == 1)
                    un, bn = (g * 2 + 1, 1) if b == 0 else (g * 2 + 2, 0)
                    for j in range(QB):
                        n = g * 8 + (4 * b + j)
                        hi_of_probs(n, j)
                        if j < QB - 1:
                            exps(g * 8 + (4 * b + j + 1), j + 1)
                        if ahead and j == 0:
                            swap_halves(un, bn, 0)
                        if ahead and j == 1:
                            hi_of_v(un, bn)
                            swap_halves(un, bn, 1)
                        if ahead and j == 2:
                            hi_of_roped(un, bn, 2)
                            swap_halves(un, bn, 3)
                        if ahead and j == 3:
                            swap_halves(un, bn, 4)
                        hi_of_o(n)
                        if ahead:
                            hi_of_roped(un, bn, (0, 1, 3, 4)[j])
                        if ahead and j == 1:
                            swap_halves(un, bn, 2)
                        if not last:
                            for p in SPLIT_AT.get((b, j), ()):
                                if p < WO_:
                                    act.wait_ge(proj_ready, (g * 2 + 1) * PROJ + (POSITION[p] + 1))
                                else:
                                    wait(act, y_ready, g * 8)
                                weight_hi(act, g + 1, p)
                        if j == QB - 1 and ahead:
                            exps(g * 8 + (4 * b + j + 1), 0)
            over_heads(act, body)

        @block.gpsimd
        def _(pool):
            pool.wait_ge(table_in, 48)

            def rotate(unit, b, i):
                par = (5 * b + i) % 2
                pool.wait_ge(swapped, unit * 5 + (i + 1))
                wait(pool, rope_split, unit * 5 + (i - 1))
                pool.tensor_tensor(roped[:, par, :], swap[:, par, :], sin[:, :], ALU.mult).then_inc(sin_part, 1)
                pool.wait_ge(sin_part, unit * 5 + (i + 1))
                k = 1 if i == 0 else i + 2
                pool.wait_ge(proj_drained, unit * PROJ + (k + 1))
                pool.tensor_tensor(roped[:, par, :], roped[:, par, :], direct[:, par, :], ALU.add).then_inc(rope_sum, 1)

            def lo_of_roped(unit, b, i):
                pool.wait_ge(rope_hi, unit * 5 + (i + 1))
                hi, lo = (k_hi[:, b, P:P + SEQ], k_lo[:, b, P:P + SEQ]) if i == 0 else (q_hi[:, b, i - 1, :], q_lo[:, b, i - 1, :])
                pool.tensor_tensor(lo, roped[:, (5 * b + i) % 2, :], hi.bitcast(F32), ALU.subtract).then_inc(rope_split, 1)

            for p in range(6):
                weight_lo(pool, 0, p)
            for i in range(5):
                rotate(0, 0, i)
                lo_of_roped(0, 0, i)
            for p in range(6, NPIECE):
                weight_lo(pool, 0, p)

            def body(g, last):
                for b in range(2):
                    ahead = not (last and b == 1)
                    un, bn = (g * 2 + 1, 1) if b == 0 else (g * 2 + 2, 0)
                    for j in range(QB):
                        if ahead:
                            if j == 0:
                                rotate(un, bn, 0)
                                lo_of_roped(un, bn, 0)
                            if j == 1:
                                rotate(un, bn, 1)
                                lo_of_roped(un, bn, 1)
                                rotate(un, bn, 2)
                            if j == 2:
                                lo_of_roped(un, bn, 2)
                                rotate(un, bn, 3)
                                lo_of_roped(un, bn, 3)
                            if j == 3:
                                rotate(un, bn, 4)
                                lo_of_roped(un, bn, 4)
                        if not last:
                            for p in SPLIT_AT.get((b, j), ()):
                                weight_lo(pool, g + 1, p)
            over_heads(pool, body)

        @block.vector
        def _(dve):
            for t in (k_hi, k_lo):
                dve.memset(t[:, :, 0:P].bitcast(F32), 0.0).then_inc(pad_done, 1)
            dve.wait_ge(table_in, 48)

            def drain_v(unit, b):
                dve.wait_ge(proj_ready, unit * PROJ + 1)
                dve.tensor_copy(v_t[:, :], ps_proj[:, (PROJ * b) % 2, :]).then_inc(proj_drained, 1)

            def lo_of_v(unit, b):
                dve.wait_ge(v_hi_done, unit + 1)
                dve.tensor_tensor(v_lo[:, b, :, :], ps_proj[:, (PROJ * b + 2) % 2, :].rearrange("p (t c) -> p t c", t=QB),
                                  v_hi[:, b, :, :].bitcast(F32), ALU.subtract).then_inc(proj_drained, 1)

            def cos_part(unit, b, i):
                k = 1 if i == 0 else i + 2
                dve.wait_ge(swapped, unit * 5 + (i + 1))
                wait(dve, rope_sum, unit * 5 + (i - 1))
                dve.tensor_tensor(direct[:, (5 * b + i) % 2, :], ps_proj[:, (PROJ * b + k) % 2, :], cos[:, :],
                                  ALU.mult).then_inc(proj_drained, 1)

            def mask_and_max(n, j):
                cols = slice(0 if j else P, 2 * P)
                for h in range(GQ):
                    if h % 2 == 0:
                        dve.wait_ge(scores_ready, n * 2 + (h // 2 + 1))
                        dve.memset(waited[:, h // 2:h // 2 + 1], 0.0).then_inc(bank_seen, 1)
                    dve.tensor_tensor_reduce(probs[:, h, cols], ps_score[:, h, cols], mask[:, cols], -SM_SCALE, 3.0e38,
                                             ALU.add, ALU.min, neg_max[:, h:h + 1]).then_inc(shifted, 1)

            def normalise(n, j):
                cols = slice(0 if j else P, 2 * P)
                dve.wait_ge(exp_done, n * GQ + GQ)
                dve.reciprocal(inv[:, :], total[:, :]).then_inc(inv_done, 1)
                dve.wait_ge(inv_done, n + 1)
                for h in range(GQ):
                    dve.tensor_scalar(probs[:, h, cols], probs[:, h, cols], inv[:, h:h + 1], None,
                                      ALU.mult).then_inc(probs_ready, 1)

            def lo_of_probs(n, j):
                dve.wait_ge(pt_hi_done, n + 1)
                w = slice(0 if j else 1, 2)
                dve.tensor_tensor(pt_lo[:, w, :], ps_pt[:, w, :], pt_hi[:, w, :].bitcast(F32), ALU.subtract).then_inc(pt_split, 1)

            def lo_of_o(n):
                dve.wait_ge(o_hi_done, n + 1)
                dve.tensor_tensor(o_lo[:, :, :], ps_o.rearrange("p (h c) -> p h c", h=GQ), o_hi[:, :, :].bitcast(F32),
                                  ALU.subtract).then_inc(o_split, 1)

            def add_y(g, n, tile):
                dve.wait_ge(y_ready, n + 1)
                if isinstance(g, int) and g == 0:
                    dve.tensor_copy(y[:, tile, :], ps_y).then_inc(y_added, 1)
                else:
                    dve.tensor_tensor(y[:, tile, :], ps_y, y[:, tile, :], ALU.add).then_inc(y_added, 1)

            drain_v(0, 0)
            cos_part(0, 0, 0)
            lo_of_v(0, 0)
            for i in range(1, 5):
                cos_part(0, 0, i)
            mask_and_max(0, 0)
            normalise(0, 0)

            def body(g, last):
                for b in range(2):
                    ahead = not (last and b == 1)
                    un, bn = (g * 2 + 1, 1) if b == 0 else (g * 2 + 2, 0)
                    for j in range(QB):
                        n = g * 8 + (4 * b + j)
                        nxt = g * 8 + (4 * b + j + 1)
                        if ahead and j == 0:
                            drain_v(un, bn)
                        lo_of_probs(n, j)
                        if j < QB - 1:
                            mask_and_max(nxt, j + 1)
                        if ahead and j == 1:
                            lo_of_v(un, bn)
                        if ahead:
                            cos_part(un, bn, (0, 1, 3, 4)[j])
                        if j < QB - 1:
                            normalise(nxt, j + 1)
                        lo_of_o(n)
                        if ahead and j == 1:
                            cos_part(un, bn, 2)
                        add_y(g, n, 4 * b + j)
                        if j == QB - 1 and ahead:
                            mask_and_max(nxt, 0)
                            normalise(nxt, 0)
            over_heads(dve, body)


def join_phase(nc, x, y, gate_dram, out):
    with ExitStack() as ctx:
        sem = lambda name: ctx.enter_context(nc.semaphore(name))
        res = ctx.enter_context(nc.sbuf_tensor("res", [P, TT, HID], F32))
        gate = ctx.enter_context(nc.sbuf_tensor("gate", [P, TT, HID], F32))
        res_in = [sem(f"res_in{t}") for t in range(TT)]
        gate_in = [sem(f"gate_in{t}") for t in range(TT)]
        product = sem("product")
        joined = sem("joined")
        stored = sem("stored")
        block = ctx.enter_context(nc.Block())

        @block.sync
        def _(sp):
            for t in range(TT):
                sp.dma_start(gate[:, t, :], gate_dram[t * P:(t + 1) * P, :]).then_inc(gate_in[t], 16)
                sp.dma_start(res[:, t, :], x[t * P:(t + 1) * P, :]).then_inc(res_in[t], 16)
            for t in range(TT):
                sp.wait_ge(joined, t + 1)
                sp.dma_start(out[t * P:(t + 1) * P, :], res[:, t, :]).then_inc(stored, 16)
            sp.wait_ge(stored, 16 * TT)

        @block.vector
        def _(dve):
            for t in range(TT):
                dve.wait_ge(gate_in[t], 16)
                dve.tensor_tensor(y[:, t, :], y[:, t, :], gate[:, t, :], ALU.mult).then_inc(product, 1)
                dve.wait_ge(product, t + 1)
                dve.wait_ge(res_in[t], 16)
                dve.tensor_tensor(res[:, t, :], res[:, t, :], y[:, t, :], ALU.add).then_inc(joined, 1)


def build(nc, a, out):
    with ExitStack() as ctx:
        sb = lambda name, shape, dt=F32: ctx.enter_context(nc.sbuf_tensor(name, shape, dt))
        ident = sb("ident_sb", [P, P])
        xt_hi = sb("xt_hi", [P, KT, TOK], F32R)
        xt_lo = sb("xt_lo", [P, KT, TOK], F32R)
        gate = nc.dram_tensor("gate_scratch", (TOK, HID), F32).ap()
        y = sb("y", [P, TT, HID])
        x = a["L0_attn_x"].rearrange("b s h -> (b s) h")
        norm_phase(nc, x, a["ident"], ident, xt_hi, xt_lo)
        ffn_phase(nc, [a[f"L0_ffn_{m}_{v}"] for m in ("gate", "up", "down") for v in "wzs"], xt_hi, xt_lo, gate)
        attention_phase(nc, a["L0_attn_wq"], a["L0_attn_wk"], a["L0_attn_wv"], a["L0_attn_wo"],
                        a["rope_cos"], a["rope_sin"], a["mask"], ident, xt_hi, xt_lo, y)
        join_phase(nc, x, y, gate, out.rearrange("b s h -> (b s) h"))


def shape_constants():
    half = P // 2
    inv_freq = (np.float32(10000.0) ** (-np.arange(half, dtype=np.float32) / np.float32(half))).astype(np.float32)
    angle = inv_freq[:, None] * np.arange(SEQ, dtype=np.float32)[None, :]
    cos, sin = np.cos(angle), np.sin(angle)
    q, c = np.arange(P)[:, None], np.arange(2 * P)[None, :]
    mask = np.where((c > q) & (c <= q + P), np.float32(0.0), np.float32(MASKED))
    return {
        "ident": np.eye(P, dtype=np.float32),
        "rope_cos": np.concatenate([cos, cos]),
        "rope_sin": np.concatenate([-sin, sin]),
        "mask": mask.astype(np.float32),
    }


def kernel(**inputs):
    import concourse.bacc as bacc
    from concourse.bass_utils import run_bass_kernel_spmd

    nc = bacc.Bacc("TRN2", target_bir_lowering=False, num_devices=1)
    arrays = {name: np.ascontiguousarray(a) for name, a in inputs.items()}
    arrays.update(shape_constants())
    aps = {name: nc.dram_tensor(name, a.shape, mybir.dt.from_np(a.dtype), kind="ExternalInput").ap()
           for name, a in arrays.items()}
    out = nc.dram_tensor("out", (BATCH, SEQ, HID), F32, kind="ExternalOutput").ap()
    build(nc, aps, out)
    r = run_bass_kernel_spmd(nc, [arrays], core_ids=[0])
    return r.results[0]["out"]
```

```python
from contextlib import ExitStack

import numpy as np
import concourse.bass as bass
from concourse import mybir

F32 = mybir.dt.float32
F32R = mybir.dt.float32r
I32 = mybir.dt.int32
ALU = mybir.AluOpType
ACT = mybir.ActivationFunctionType

P = 128
BATCH, SEQ, HID = 2, 512, 512
TOK = BATCH * SEQ
KT = HID // P
TT = TOK // P
QB = SEQ // P
NKV, GQ = 8, 4
INTER = 1792
NI = INTER // P
PAIRS = NI // 2
EPS = 1e-5
SM_SCALE = float(P) ** -0.5
MASKED = -3.0e38


def wait(eng, sem, count):
    if isinstance(count, int) and count <= 0:
        return
    eng.wait_ge(sem, count)


def three_passes(pe, out, stat, mov, first, last):
    pe.matmul(out, stat[1], mov[0], start=first, stop=False)
    pe.matmul(out, stat[0], mov[1], start=False, stop=False)
    return pe.matmul(out, stat[0], mov[0], start=False, stop=last)


class Shared:

    WORK = 11
    ROPE_AT = 5
    RING, DQ = 3, 2

    def __init__(self, nc, ctx):
        sb = lambda name, shape, dt=F32: ctx.enter_context(nc.sbuf_tensor(name, shape, dt))
        sem = lambda name: ctx.enter_context(nc.semaphore(name))
        self.ident = sb("ident_sb", [P, P])
        self.xt_hi = sb("xt_hi", [P, KT, TOK], F32R)
        self.xt_lo = sb("xt_lo", [P, KT, TOK], F32R)
        self.y = sb("y", [P, TT, HID])
        self.work = sb("work", [P, self.WORK, 512])
        self.w_hi = sb("w_hi", [P, 6, KT, P], F32R)
        self.w_lo = sb("w_lo", [P, 6, KT, P], F32R)
        self.ps = ctx.enter_context(nc.psum_tensor("ps", [P, 8, 512], F32))
        self.raw_in = [sem(f"ffn_raw_in{s}") for s in range(self.RING)]
        self.zero_off = sem("zero_off")
        self.scaled = sem("scaled")
        self.w_hi_done = sem("ffn_w_hi_done")
        self.w_split = sem("ffn_w_split")
        self.gu_ready = sem("gu_ready")

    def raw(self, s):
        w, z, sc = (self.work[:, 3 * s + i, :] for i in range(3))
        return w.bitcast(I32), z.bitcast(I32), sc

    def dq(self, q):
        return self.work[:, 3 * self.RING + q, :]

    def gate_up(self, pe, e, kind):
        ii, hf = ORDER[e]
        s, cols = FfnWeights.slot_of(kind, ii), slice(hf * 512, (hf + 1) * 512)
        for k in range(KT):
            last = three_passes(pe, self.ps[:, 2 * (e % 2) + kind, :], (self.w_hi[:, s, k, :], self.w_lo[:, s, k, :]),
                                (self.xt_hi[:, k, cols], self.xt_lo[:, k, cols]), k == 0, k == KT - 1)
        last.then_inc(self.gu_ready, 1)


GATE, UP, DOWN = 0, 1, 2
ORDER = [(0, 0), (1, 0), (0, 1), (1, 1)]
AHEAD = [(GATE, 0), (UP, 0), (GATE, 1), (UP, 1)]
IN_BODY = [(DOWN, 0), (DOWN, 1)] + AHEAD


class FfnWeights:

    def __init__(self, sh, weights):
        self.sh, self.weights = sh, weights

    @staticmethod
    def slot_of(kind, ii):
        return 4 + ii if kind == DOWN else 2 * ii + kind

    @staticmethod
    def index(n, at):
        return n * 6 + (4 + at)

    @staticmethod
    def piece(at):
        return AHEAD[at + 4] if at < 0 else IN_BODY[at]

    @staticmethod
    def ring_slot(at):
        return (4 + at) % Shared.RING

    def load(self, eng, n, at, kind, ii, pair):
        sh, s = self.sh, self.ring_slot(at)
        gate_w, gate_z, gate_s, up_w, up_z, up_s, down_w, down_z, down_s = self.weights
        to_w, to_z, to_s = sh.raw(s)
        wait(eng, sh.w_split, self.index(n, at) - sh.RING + 1)
        cols = bass.ds(pair * (2 * P) + ii * P, P)
        if kind == DOWN:
            row = bass.ds(pair * 2 + ii, 1)
            spread = lambda t: t[row, :].rearrange("a c -> (a c)").partition_broadcast(P)
            eng.dma_start(to_w, down_w[cols, :]).then_inc(sh.raw_in[s], 16)
            eng.dma_start(to_z, spread(down_z)).then_inc(sh.raw_in[s], 16)
            eng.dma_start(to_s, spread(down_s)).then_inc(sh.raw_in[s], 16)
        else:
            w, z, sc = (gate_w, gate_z, gate_s) if kind == GATE else (up_w, up_z, up_s)
            cut = lambda t: t.rearrange("p (k c) -> p k c", k=KT)
            eng.dma_start(cut(to_w), w[:, cols].rearrange("(k p) c -> p k c", p=P)).then_inc(sh.raw_in[s], 16)
            eng.dma_start(cut(to_z), z[:, cols].partition_broadcast(P)).then_inc(sh.raw_in[s], 16)
            eng.dma_start(cut(to_s), sc[:, cols].partition_broadcast(P)).then_inc(sh.raw_in[s], 16)

    def dequantise(self, dve, n, at):
        sh, s, q = self.sh, self.ring_slot(at), at % Shared.DQ
        k = self.index(n, at)
        w, z, sc = sh.raw(s)
        dve.wait_ge(sh.raw_in[s], (n * 2 + ((4 + at) // sh.RING + 1)) * 48)
        wait(dve, sh.w_split, k - sh.DQ + 1)
        dve.tensor_tensor(sh.dq(q), w, z, ALU.subtract).then_inc(sh.zero_off, 1)
        dve.wait_ge(sh.zero_off, k + 1)
        dve.tensor_tensor(sh.dq(q), sh.dq(q), sc, ALU.mult).then_inc(sh.scaled, 1)

    def target(self, kind, ii):
        flat = lambda w: w[:, self.slot_of(kind, ii), :, :].rearrange("p k c -> p (k c)")
        return flat(self.sh.w_hi), flat(self.sh.w_lo)

    def hi(self, act, n, at, kind, ii):
        act.wait_ge(self.sh.scaled, self.index(n, at) + 1)
        act.activation(self.target(kind, ii)[0], self.sh.dq(at % Shared.DQ), ACT.Copy).then_inc(self.sh.w_hi_done, 1)

    def lo(self, pool, n, at, kind, ii):
        hi, lo = self.target(kind, ii)
        pool.wait_ge(self.sh.w_hi_done, self.index(n, at) + 1)
        pool.tensor_tensor(lo, self.sh.dq(at % Shared.DQ), hi.bitcast(F32), ALU.subtract).then_inc(self.sh.w_split, 1)


def ffn_block(nc, sh, fw, x, out):
    gu_ready = sh.gu_ready
    with ExitStack() as ctx:
        sb = lambda name, shape, dt=F32: ctx.enter_context(nc.sbuf_tensor(name, shape, dt))
        sem = lambda name: ctx.enter_context(nc.semaphore(name))
        sil = sb("sil", [P, 2, 512])
        mid = sb("mid", [P, 2, 512])
        mid_hi = sb("mid_hi", [P, 2, TOK], F32R)
        mid_lo = sb("mid_lo", [P, 2, TOK], F32R)
        acc = sb("ffn_acc", [P, TT, HID])
        res = sb("res", [P, TT, HID])
        ps = sh.ps
        ps_down = ps[:, 4:8, :]
        silu_done = sem("silu_done")
        mid_done = sem("mid_done")
        mid_hi_done = sem("mid_hi_done")
        mid_split = sem("mid_split")
        down_ready = sem("down_ready")
        acc_done = sem("acc_done")
        res_in = sem("res_in")
        gate_done = sem("gate_done")
        gated = sem("gated")
        last_gated = sem("last_gated")
        joined = sem("joined")
        stored = sem("stored")
        block = ctx.enter_context(nc.Block())

        def pieces(at0, at1):
            return [(at, *IN_BODY[at]) for at in range(at0, at1)]

        def first(n):
            return isinstance(n, int) and n == 0

        def over_pairs(eng, body):
            body(0, False)
            with eng.Fori(1, PAIRS - 1) as n:
                body(n, False)
            body(PAIRS - 1, True)

        @block.sync
        def _(sp):
            def body(n, last):
                for at, kind, ii in pieces(2 if first(n) else 0, 2 if last else 6):
                    fw.load(sp, n, at, kind, ii, n if at < 2 else n + 1)
            over_pairs(sp, body)
            sp.dma_start(res[:, :, :], x.rearrange("(t p) h -> p t h", p=P)).then_inc(res_in, 16)
            for t in range(TT):
                sp.wait_ge(joined, t + 1)
                sp.dma_start(out[t * P:(t + 1) * P, :], res[:, t, :]).then_inc(stored, 16)
            sp.wait_ge(stored, 16 * TT)

        @block.tensor
        def _(pe):
            def gate_up(n, e):
                ii = ORDER[e][0]
                for kind in (GATE, UP):
                    wait(pe, sh.w_split, fw.index(n, 2 * ii + kind - 4) + 1)
                    if kind == GATE:
                        wait(pe, silu_done, n * 4 + (e - 1))
                    else:
                        wait(pe, mid_done, n * 4 + (e - 1))
                    sh.gate_up(pe, e, kind)

            def down(n, t):
                pe.wait_ge(mid_split, n * 4 + (2 if t < TT // 2 else 4))
                wait(pe, sh.w_split, fw.index(n, 0) + 2)
                wait(pe, acc_done, n * TT + (t - 4 + 1))
                for ii in range(2):
                    last = three_passes(pe, ps_down[:, t % 4, :],
                                        (mid_hi[:, ii, t * P:(t + 1) * P], mid_lo[:, ii, t * P:(t + 1) * P]),
                                        fw.target(DOWN, ii), ii == 0, ii == 1)
                last.then_inc(down_ready, 1)

            def body(n, last):
                for e in range(2 if first(n) else 0, 4):
                    gate_up(n, e)
                for t in range(TT):
                    down(n, t)
            over_pairs(pe, body)

        @block.scalar
        def _(act):
            def silu(n, e):
                ii, hf = ORDER[e]
                act.wait_ge(gu_ready, n * 8 + (2 * e + 1))
                wait(act, mid_done, n * 4 + (e - 1))
                act.activation(sil[:, e % 2, :], ps[:, 2 * (e % 2) + GATE, :], ACT.Silu).then_inc(silu_done, 1)
                act.wait_ge(mid_done, n * 4 + (e + 1))
                act.activation(mid_hi[:, ii, hf * 512:(hf + 1) * 512], mid[:, e % 2, :], ACT.Copy).then_inc(mid_hi_done, 1)

            def body(n, last):
                for e in range(4):
                    silu(n, e)
                    if e == 1 and not first(n):
                        wait(act, down_ready, n * TT)
                        for at, kind, ii in pieces(0, 2):
                            fw.hi(act, n, at, kind, ii)
                    if not last and e >= 2:
                        for at, kind, ii in pieces(2 * e - 2, 2 * e):
                            fw.hi(act, n, at, kind, ii)
            over_pairs(act, body)
            for t in range(TT):
                act.wait_ge(acc_done, TT * (PAIRS - 1) + t + 1)
                act.activation(acc[:, t, :], acc[:, t, :], ACT.Silu).then_inc(gate_done, 1)

        @block.gpsimd
        def _(pool):
            def split_mid(n, e):
                ii, hf = ORDER[e]
                pool.wait_ge(mid_hi_done, n * 4 + (e + 1))
                cols = slice(hf * 512, (hf + 1) * 512)
                pool.tensor_tensor(mid_lo[:, ii, cols], mid[:, e % 2, :], mid_hi[:, ii, cols].bitcast(F32),
                                   ALU.subtract).then_inc(mid_split, 1)

            def body(n, last):
                for e in range(4):
                    split_mid(n, e)
                    if e == 1 and not first(n):
                        for at, kind, ii in pieces(0, 2):
                            fw.lo(pool, n, at, kind, ii)
                    if not last and e >= 2:
                        for at, kind, ii in pieces(2 * e - 2, 2 * e):
                            fw.lo(pool, n, at, kind, ii)
            over_pairs(pool, body)
            for t in range(TT - 1):
                pool.wait_ge(gate_done, t + 1)
                pool.tensor_tensor(acc[:, t, :], acc[:, t, :], sh.y[:, t, :], ALU.mult).then_inc(gated, 1)

        @block.vector
        def _(dve):
            def middle(n, e):
                dve.wait_ge(gu_ready, n * 8 + (2 * e + 2))
                dve.wait_ge(silu_done, n * 4 + (e + 1))
                wait(dve, mid_split, n * 4 + (e - 1))
                dve.tensor_tensor(mid[:, e % 2, :], sil[:, e % 2, :], ps[:, 2 * (e % 2) + UP, :], ALU.mult).then_inc(mid_done, 1)

            def join(t):
                if t == 0:
                    dve.wait_ge(res_in, 16)
                if t == TT - 1:
                    dve.wait_ge(gate_done, TT)
                    dve.tensor_tensor(acc[:, t, :], acc[:, t, :], sh.y[:, t, :], ALU.mult).then_inc(last_gated, 1)
                    dve.wait_ge(last_gated, 1)
                else:
                    dve.wait_ge(gated, t + 1)
                dve.tensor_tensor(res[:, t, :], acc[:, t, :], res[:, t, :], ALU.add).then_inc(joined, 1)

            def body(n, last):
                for e in range(4):
                    middle(n, e)
                    if e == 1 and not first(n):
                        for at in range(2):
                            fw.dequantise(dve, n, at)
                    if not last and e >= 2:
                        for at in range(2 * e - 2, 2 * e):
                            fw.dequantise(dve, n, at)
                for t in range(TT):
                    dve.wait_ge(down_ready, n * TT + (t + 1))
                    if first(n):
                        dve.tensor_copy(acc[:, t, :], ps_down[:, t % 4, :]).then_inc(acc_done, 1)
                    else:
                        dve.tensor_tensor(acc[:, t, :], ps_down[:, t % 4, :], acc[:, t, :], ALU.add).then_inc(acc_done, 1)
                    if last and t >= 2:
                        join(t - 2)
            over_pairs(dve, body)
            for t in range(TT - 2, TT):
                join(t)


def attention_block(nc, sh, fw, x, wq, wk, wv, wo, cos_in, sin_in, mask_in, ident_in):
    K_, Q_, V_, WO_ = 0, 1, 5, 6
    NPIECE = 10
    RING = 5
    UNITS = NKV * BATCH
    ident, xt_hi, xt_lo, y, w_hi, w_lo = sh.ident, sh.xt_hi, sh.xt_lo, sh.y, sh.w_hi, sh.w_lo
    raw = [sh.work[:, s, :] for s in range(RING)]
    swap, direct, roped = (sh.work[:, Shared.ROPE_AT + 2 * i:Shared.ROPE_AT + 2 * i + 2, :] for i in range(3))
    xin = y
    PROJ = 7
    TURN = 6
    with ExitStack() as ctx:
        sb = lambda name, shape, dt=F32: ctx.enter_context(nc.sbuf_tensor(name, shape, dt))
        sem = lambda name: ctx.enter_context(nc.semaphore(name))
        cos = sb("cos", [P, SEQ])
        sin = sb("sin", [P, SEQ])
        mask = sb("mask_sb", [P, 2 * P])
        wo_hi = sb("wo_hi", [P, 2 * GQ * HID], F32R)
        wo_lo = sb("wo_lo", [P, 2 * GQ * HID], F32R)
        q_hi = sb("q_hi", [P, 2, GQ, SEQ], F32R)
        q_lo = sb("q_lo", [P, 2, GQ, SEQ], F32R)
        k_hi = sb("k_hi", [P, 2, P + SEQ], F32R)
        k_lo = sb("k_lo", [P, 2, P + SEQ], F32R)
        v_t = sb("v_t", [P, SEQ])
        v_hi = sb("v_hi", [P, 2, QB, P], F32R)
        v_lo = sb("v_lo", [P, 2, QB, P], F32R)
        probs = sb("probs", [P, GQ, 2 * P])
        neg_max = sb("neg_max", [P, GQ])
        total = sb("total", [P, GQ])
        waited = sb("waited", [P, 2])
        preload = sb("preload", [P, 2])
        inv = sb("inv", [P, GQ])
        pt_hi = sb("pt_hi", [P, 2, GQ * P], F32R)
        pt_lo = sb("pt_lo", [P, 2, GQ * P], F32R)
        o_hi = sb("o_hi", [P, 2, GQ, P], F32R)
        o_lo = sb("o_lo", [P, 2, GQ, P], F32R)
        stats = sb("stats", [P, TT, 6])
        mv = sb("mv", [P, TT, 2])
        var, root, r0, r2, corr, rstd = (sb(name, [P, TT]) for name in ("var", "root", "r0", "r2", "corr", "rstd"))
        ps = sh.ps
        ps_proj = ps[:, 0:2, :]
        ps_score = ps[:, 2:4, :].rearrange("p a (h c) -> p (a h) c", h=2)
        ps_pt = ps[:, 4:6, :]
        ps_o = ps[:, 6, :]
        ps_y = ps[:, 7, :]

        x_in = [sem(f"x_in{t}") for t in range(TT)]
        ident_ld = sem("ident_ld")
        stat_done = sem("stat_done")
        var_done = sem("var_done")
        root_done = sem("root_done")
        newton = sem("newton")
        xn_done = sem("xn_done")
        turned = sem("turned")
        xt_hi_done = sem("xt_hi_done")
        xt_done = sem("xt_done")
        y_zeroed = sem("y_zeroed")
        table_in = sem("table_in")
        pad_done = sem("pad_done")
        raw_in = [sem(f"att_raw_in{s}") for s in range(RING)]
        w_hi_done = sem("w_hi_done")
        w_split = sem("w_split")
        proj_ready = sem("proj_ready")
        proj_drained = sem("proj_drained")
        v_hi_done = sem("v_hi_done")
        swapped = sem("swapped")
        sin_part = sem("sin_part")
        rope_sum = sem("rope_sum")
        rope_hi = sem("rope_hi")
        rope_split = sem("rope_split")
        scores_ready = sem("scores_ready")
        shifted = sem("shifted")
        bank_seen = sem("bank_seen")
        exp_done = sem("exp_done")
        inv_done = sem("inv_done")
        probs_ready = sem("probs_ready")
        pt_ready = sem("pt_ready")
        pt_hi_done = sem("pt_hi_done")
        pt_split = sem("pt_split")
        o_ready = sem("o_ready")
        o_hi_done = sem("o_hi_done")
        o_split = sem("o_split")
        y_ready = sem("y_ready")
        y_added = sem("y_added")
        block = ctx.enter_context(nc.Block())

        def over_heads(eng, body):
            body(0, False)
            with eng.Fori(1, NKV - 1) as g:
                body(g, False)
            body(NKV - 1, True)

        def load_weight(eng, g, p):
            s = p % RING
            wait(eng, w_split, g * NPIECE + (p - RING + 1))
            if p >= WO_:
                src = wo[bass.ds(g * (GQ * P) + (p - WO_) * P, P), :]
                dst = raw[s][:, :]
            else:
                w, col = (wk, g * P) if p == K_ else (wv, g * P) if p == V_ else (wq, g * (GQ * P) + (p - Q_) * P)
                src = w[:, bass.ds(col, P)].rearrange("(k p) c -> p k c", p=P)
                dst = raw[s][:, :].rearrange("p (k c) -> p k c", k=KT)
            eng.dma_start(dst, src).then_inc(raw_in[s], 16)

        def split_target(g, p):
            if p < WO_:
                flat = lambda w: w[:, p, :, :].rearrange("p k c -> p (k c)")
                return flat(w_hi), flat(w_lo)
            half = (g & 1) * (GQ * HID)
            at = bass.ds(half + (p - WO_) * HID, HID)
            return wo_hi[:, at], wo_lo[:, at]

        def weight_hi(act, g, p):
            act.wait_ge(raw_in[p % RING], g * 32 + (p // RING + 1) * 16)
            act.activation(split_target(g, p)[0], raw[p % RING][:, :], ACT.Copy).then_inc(w_hi_done, 1)

        def weight_lo(pool, g, p):
            pool.wait_ge(w_hi_done, g * NPIECE + (p + 1))
            hi, lo = split_target(g, p)
            pool.tensor_tensor(lo, raw[p % RING][:, :], hi.bitcast(F32), ALU.subtract).then_inc(w_split, 1)

        SPLIT_AT = {(0, 1): (0, 1), (0, 2): (2, 3), (0, 3): (4, 5), (1, 0): (6,), (1, 1): (7,), (1, 2): (8,), (1, 3): (9,)}
        FFN_AT = ((-4,), (-3,), (-2,), (-1, 0, 1))
        bank = lambda b, k: ps_proj[:, (PROJ * b + k) % 2, :]
        GROUP = TT // 2

        @block.sync
        def _(sp):
            def load_x(tiles):
                for t in tiles:
                    sp.dma_start(xin[:, t, :], x[t * P:(t + 1) * P, :]).then_inc(x_in[t], 16)
            load_x(range(0, GROUP, 2))
            for p in range(2):
                load_weight(sp, 0, p)
            load_x(range(GROUP, TT, 2))
            sp.dma_start(cos[:, :], cos_in).then_inc(table_in, 16)
            sp.dma_start(sin[:, :], sin_in).then_inc(table_in, 16)
            sp.dma_start(mask[:, :], mask_in).then_inc(table_in, 16)
            for p in range(2, NPIECE):
                load_weight(sp, 0, p)

            def body(g, last):
                if not last:
                    for p in range(NPIECE):
                        load_weight(sp, g + 1, p)
            over_heads(sp, body)
            sp.wait_ge(w_split, NKV * NPIECE)
            for at in range(-4, 2):
                if at == -3:
                    sp.wait_ge(rope_split, UNITS * 5)
                fw.load(sp, 0, at, *fw.piece(at), 0)

        @block.tensor
        def _(pe):
            def project(g, unit, b, k):
                if k == TURN:
                    return turn_v(unit, b)
                wait(pe, w_split, g * NPIECE + (k + 1))
                wait(pe, proj_drained, unit * PROJ + (k - 1))
                for t in range(KT):
                    cols = slice(b * SEQ, (b + 1) * SEQ)
                    last = three_passes(pe, bank(b, k), (w_hi[:, k, t, :], w_lo[:, k, t, :]),
                                        (xt_hi[:, t, cols], xt_lo[:, t, cols]), t == 0, t == KT - 1)
                last.then_inc(proj_ready, 1)

            def turn_v(unit, b):
                pe.wait_ge(proj_drained, unit * PROJ + TURN)
                for t in range(QB):
                    last = pe.transpose(bank(b, TURN)[:, t * P:(t + 1) * P], v_t[:, t * P:(t + 1) * P], ident[:, :])
                last.then_inc(proj_ready, 1)

            def scores(n, unit, b, j, heads=range(GQ)):
                wait(pe, shifted, n * GQ)
                for h in heads:
                    wait(pe, rope_split, unit * 5 + (h + 2))
                    q = [t[:, b, h, j * P:(j + 1) * P] for t in (q_hi, q_lo)]
                    k = [t[:, b, j * P:(j + 2) * P] for t in (k_hi, k_lo)]
                    last = three_passes(pe, ps_score[:, h, :], q, k, True, True)
                    if h % 2:
                        last.then_inc(scores_ready, 1)

            def turn_probs(n, j):
                wait(pe, pt_split, n)
                for h in range(GQ):
                    pe.wait_ge(probs_ready, n * GQ + (h + 1))
                    for w in range(0 if j else 1, 2):
                        last = pe.transpose(ps_pt[:, w, h * P:(h + 1) * P], probs[:, h, w * P:(w + 1) * P], ident[:, :])
                last.then_inc(pt_ready, 1)

            def weigh_values(n, unit, b, j):
                pe.wait_ge(pt_split, n + 1)
                pe.wait_ge(proj_drained, unit * PROJ + PROJ)
                wait(pe, o_split, n)
                windows = range(0 if j else 1, 2)
                for w in windows:
                    v = [t[:, b, j - 1 + w, :] for t in (v_hi, v_lo)]
                    last = three_passes(pe, ps_o[:, :], v, (pt_hi[:, w, :], pt_lo[:, w, :]), w == windows[0], w == 1)
                last.then_inc(o_ready, 1)

            def project_out(g, b, j):
                if (b, j) == (0, 0):
                    if isinstance(g, int) and g == 0:
                        return
                    owner = g + 1
                else:
                    owner = g
                    wait(pe, w_split, g * NPIECE + NPIECE)
                n = g * 8 + (4 * b + j)
                pe.wait_ge(o_split, n)
                wait(pe, y_added, n - 1)
                par = (j - 1) % 2
                for h in range(GQ):
                    last = three_passes(pe, ps_y[:, :], (o_hi[:, par, h, :], o_lo[:, par, h, :]),
                                        split_target(owner, WO_ + h), h == 0, h == GQ - 1)
                last.then_inc(y_ready, 1)

            def turn_x(group):
                for t in range(group * GROUP, (group + 1) * GROUP):
                    pe.wait_ge(xn_done, t + 1)
                    for k in range(KT):
                        last = pe.transpose(ps[:, t, k * P:(k + 1) * P], xin[:, t, k * P:(k + 1) * P], ident[:, :])
                    last.then_inc(turned, 1)

            def ffn_product(e, kind):
                if e == 1:
                    pe.wait_ge(shifted, UNITS * QB * GQ)
                pe.wait_ge(sh.w_split, 2 * e + kind + 1)
                sh.gate_up(pe, e, kind)

            pe.wait_ge(ident_ld, 16)
            turn_x(0)
            pe.wait_ge(xt_done, GROUP)
            for k in range(TURN):
                if k == 3:
                    turn_x(1)
                project(0, 0, 0, k)
            pe.wait_ge(pad_done, 2)
            scores(0, 0, 0, 0, range(0, 2))
            project(0, 0, 0, TURN)
            pe.wait_ge(xt_done, TT)
            project(0, 1, 1, 0)
            scores(0, 0, 0, 0, range(2, GQ))

            def body(g, last):
                for b in range(2):
                    unit = g * 2 + b
                    ahead = not (last and b == 1)
                    gn, un, bn = (g, g * 2 + 1, 1) if b == 0 else (g + 1, g * 2 + 2, 0)

                    def ahead_project(*ks):
                        if ahead:
                            for k in ks:
                                project(gn, un, bn, k)
                    for j in range(QB):
                        n = g * 8 + (4 * b + j)
                        if j == 0 and not (isinstance(g, int) and (g, b) == (0, 0)):
                            ahead_project(0)
                        turn_probs(n, j)
                        if j < QB - 1:
                            scores(g * 8 + (4 * b + j + 1), unit, b, j + 1)
                        ahead_project(*((1,), (2,), (4, 5), (6,))[j])
                        if not ahead and j == 3:
                            ffn_product(1, GATE)
                        project_out(g, b, j)
                        if j == QB - 1 and ahead:
                            scores(g * 8 + (4 * b + j + 1), un, bn, 0)
                        weigh_values(n, unit, b, j)
                        if j == 1:
                            ahead_project(3)
                        if not ahead and j == 1:
                            ffn_product(0, GATE)
                        if not ahead and j >= 2:
                            ffn_product(j - 2, UP)
            over_heads(pe, body)
            project_out(NKV - 1, 1, QB)

        @block.scalar
        def _(act):
            def swap_halves(unit, b, i):
                par = (5 * b + i) % 2
                act.wait_ge(proj_ready, unit * PROJ + (i + 1))
                wait(act, rope_sum, unit * 5 + (i - 1))
                src = bank(b, i)
                act.activation(swap[0:P // 2, par, :], src[P // 2:P, :], ACT.Copy)
                act.activation(swap[P // 2:P, par, :], src[0:P // 2, :], ACT.Copy).then_inc(swapped, 1)

            def rope_target(b, i):
                return (k_hi[:, b, P:P + SEQ], k_lo[:, b, P:P + SEQ]) if i == 0 else (q_hi[:, b, i - 1, :], q_lo[:, b, i - 1, :])

            def hi_of_roped(unit, b, i):
                act.wait_ge(rope_sum, unit * 5 + (i + 1))
                act.activation(rope_target(b, i)[0], roped[:, (5 * b + i) % 2, :], ACT.Copy).then_inc(rope_hi, 1)

            def hi_of_v(unit, b):
                act.wait_ge(proj_ready, unit * PROJ + PROJ)
                act.activation(v_hi[:, b, :, :], bank(b, TURN).rearrange("p (t c) -> p t c", t=QB),
                               ACT.Copy).then_inc(v_hi_done, 1)

            def exps(n, j):
                cols = slice(0 if j else P, 2 * P)
                for h in range(GQ):
                    act.wait_ge(shifted, n * GQ + (h + 1))
                    act.activation(probs[:, h, cols], probs[:, h, cols], ACT.Exp, scale=-1.0, bias=neg_max[:, h:h + 1],
                                   accum_out=total[:, h:h + 1]).then_inc(exp_done, 1)

            def hi_of_probs(n, j):
                act.wait_ge(pt_ready, n + 1)
                w = slice(0 if j else 1, 2)
                act.activation(pt_hi[:, w, :], ps_pt[:, w, :], ACT.Copy).then_inc(pt_hi_done, 1)

            def hi_of_o(n, j):
                act.wait_ge(o_ready, n + 1)
                act.activation(o_hi[:, j % 2, :, :], ps_o.rearrange("p (h c) -> p h c", h=GQ), ACT.Copy).then_inc(o_hi_done, 1)

            def root_of_var(group):
                cols = slice(group * GROUP, (group + 1) * GROUP)
                act.wait_ge(var_done, TT // 2 * (group + 1) + group + 1)
                act.activation(root[:, cols], var[:, cols], ACT.Sqrt).then_inc(root_done, 1)

            def hi_of_x(group):
                for t in range(group * GROUP, (group + 1) * GROUP):
                    act.wait_ge(turned, t + 1)
                    act.activation(xt_hi[:, :, t * P:(t + 1) * P],
                                   ps[:, t, :].rearrange("p (k c) -> p k c", k=KT), ACT.Copy).then_inc(xt_hi_done, 1)

            for t in range(1, TT, 2):
                act.dma_start(xin[:, t, :], x[t * P:(t + 1) * P, :]).then_inc(x_in[t], 16)
                if t == GROUP - 1:
                    act.dma_start(ident[:, :], ident_in).then_inc(ident_ld, 16)
            root_of_var(0)
            for p in range(2):
                weight_hi(act, 0, p)
            hi_of_x(0)
            for p in range(2, 6):
                weight_hi(act, 0, p)
            swap_halves(0, 0, 0)
            root_of_var(1)
            act.wait_ge(root_done, 2)
            act.activation(preload[:, 0:1], root[:, 0:1], ACT.Exp)
            swap_halves(0, 0, 1)
            hi_of_roped(0, 0, 0)
            swap_halves(0, 0, 2)
            hi_of_roped(0, 0, 1)
            hi_of_x(1)
            hi_of_roped(0, 0, 2)
            swap_halves(0, 0, 3)
            hi_of_roped(0, 0, 3)
            swap_halves(0, 0, 4)
            for p in range(6, 8):
                weight_hi(act, 0, p)
            hi_of_roped(0, 0, 4)
            exps(0, 0)
            for p in range(8, 10):
                weight_hi(act, 0, p)
            hi_of_v(0, 0)

            def body(g, last):
                for b in range(2):
                    ahead = not (last and b == 1)
                    un, bn = (g * 2 + 1, 1) if b == 0 else (g * 2 + 2, 0)
                    for j in range(QB):
                        n = g * 8 + (4 * b + j)
                        if ahead and j == 0:
                            swap_halves(un, bn, 0)
                        hi_of_probs(n, j)
                        if ahead and j == 2:
                            hi_of_roped(un, bn, 3)
                        if ahead and j == 3:
                            hi_of_v(un, bn)
                        if j < QB - 1:
                            exps(g * 8 + (4 * b + j + 1), j + 1)
                        elif ahead:
                            exps(g * 8 + (4 * b + j + 1), 0)
                        if ahead and j == 0:
                            hi_of_roped(un, bn, 0)
                            swap_halves(un, bn, 1)
                        if ahead and j == 1:
                            swap_halves(un, bn, 2)
                        if ahead and j == 2:
                            swap_halves(un, bn, 4)
                        if not ahead:
                            act.wait_ge(proj_ready, UNITS * PROJ)
                            for at in FFN_AT[j]:
                                fw.hi(act, 0, at, *fw.piece(at))
                        hi_of_o(n, j)
                        if ahead and j < 3:
                            hi_of_roped(un, bn, (1, 2, 4)[j])
                        if ahead and j == 1:
                            swap_halves(un, bn, 3)
                        if not last:
                            for p in SPLIT_AT.get((b, j), ()):
                                if p < WO_:
                                    act.wait_ge(proj_ready, (g * 2 + 1) * PROJ + (p + 1))
                                else:
                                    wait(act, y_ready, g * 8)
                                weight_hi(act, g + 1, p)
            over_heads(act, body)
            act.activation(preload[:, 1:2], root[:, 0:1], ACT.Silu)

        @block.gpsimd
        def _(pool):
            def times_sin(unit, b, i):
                par = (5 * b + i) % 2
                pool.wait_ge(swapped, unit * 5 + (i + 1))
                wait(pool, rope_split, unit * 5 + (i - 1))
                pool.tensor_tensor(roped[:, par, :], swap[:, par, :], sin[:, :], ALU.mult).then_inc(sin_part, 1)

            def rotate(unit, b, i):
                par = (5 * b + i) % 2
                times_sin(unit, b, i)
                pool.wait_ge(sin_part, unit * 5 + (i + 1))
                pool.wait_ge(proj_drained, unit * PROJ + (i + 1))
                pool.tensor_tensor(roped[:, par, :], roped[:, par, :], direct[:, par, :], ALU.add).then_inc(rope_sum, 1)

            def lo_of_roped(unit, b, i):
                pool.wait_ge(rope_hi, unit * 5 + (i + 1))
                hi, lo = (k_hi[:, b, P:P + SEQ], k_lo[:, b, P:P + SEQ]) if i == 0 else (q_hi[:, b, i - 1, :], q_lo[:, b, i - 1, :])
                pool.tensor_tensor(lo, roped[:, (5 * b + i) % 2, :], hi.bitcast(F32), ALU.subtract).then_inc(rope_split, 1)

            for p in range(2):
                weight_lo(pool, 0, p)
            pool.wait_ge(table_in, 48)
            for p in range(2, 6):
                weight_lo(pool, 0, p)
            for i in range(5):
                times_sin(0, 0, i)
                if i > 0:
                    lo_of_roped(0, 0, i - 1)
            lo_of_roped(0, 0, 4)
            for p in range(WO_, NPIECE):
                weight_lo(pool, 0, p)
            pool.wait_ge(turned, TT)
            pool.memset(y[:, TT - 1, :], 0.0).then_inc(y_zeroed, 1)

            def body(g, last):
                for b in range(2):
                    ahead = not (last and b == 1)
                    un, bn = (g * 2 + 1, 1) if b == 0 else (g * 2 + 2, 0)
                    for j in range(QB):
                        if ahead and j == 0:
                            rotate(un, bn, 0)
                            lo_of_roped(un, bn, 0)
                        if ahead and j < 2:
                            rotate(un, bn, j + 1)
                            lo_of_roped(un, bn, j + 1)
                        if ahead and j == 1:
                            rotate(un, bn, 3)
                        if ahead and j == 2:
                            lo_of_roped(un, bn, 3)
                            rotate(un, bn, 4)
                            lo_of_roped(un, bn, 4)
                        if not last:
                            for p in SPLIT_AT.get((b, j), ()):
                                weight_lo(pool, g + 1, p)
                        if not ahead:
                            for at in FFN_AT[j]:
                                fw.lo(pool, 0, at, *fw.piece(at))
            over_heads(pool, body)

        @block.vector
        def _(dve):
            for t in (k_hi, k_lo):
                dve.memset(t[:, :, 0:P].bitcast(F32), 0.0).then_inc(pad_done, 1)

            def statistics(tiles):
                for t in tiles:
                    dve.wait_ge(x_in[t], 16)
                    dve.bn_stats(stats[:, t, :], xin[:, t, :]).then_inc(stat_done, 1)
                for t in tiles:
                    dve.wait_ge(stat_done, t + 1)
                    dve.bn_aggr(mv[:, t, :], stats[:, t, :]).then_inc(var_done, 1)

            def variance(group):
                c = slice(group * GROUP, (group + 1) * GROUP)
                dve.wait_ge(var_done, GROUP * (group + 1) + group)
                dve.tensor_scalar(var[:, c], mv[:, c, 1], EPS, None, ALU.add).then_inc(var_done, 1)

            def normed(group):
                c = slice(group * GROUP, (group + 1) * GROUP)
                done = 5 * group
                dve.wait_ge(root_done, group + 1)
                dve.reciprocal(r0[:, c], root[:, c]).then_inc(newton, 1)
                dve.wait_ge(newton, done + 1)
                dve.tensor_tensor(r2[:, c], r0[:, c], r0[:, c], ALU.mult).then_inc(newton, 1)
                dve.wait_ge(newton, done + 2)
                dve.tensor_tensor(corr[:, c], r2[:, c], var[:, c], ALU.mult).then_inc(newton, 1)
                dve.wait_ge(newton, done + 3)
                dve.tensor_scalar(r2[:, c], corr[:, c], -0.5, 1.5, ALU.mult, ALU.add).then_inc(newton, 1)
                dve.wait_ge(newton, done + 4)
                dve.tensor_tensor(rstd[:, c], r0[:, c], r2[:, c], ALU.mult).then_inc(newton, 1)
                dve.wait_ge(newton, done + 5)
                for t in range(group * GROUP, (group + 1) * GROUP):
                    dve.tensor_scalar(xin[:, t, :], xin[:, t, :], mv[:, t, 0:1], rstd[:, t:t + 1],
                                      ALU.subtract, ALU.mult).then_inc(xn_done, 1)

            def lo_of_x(group):
                for t in range(group * GROUP, (group + 1) * GROUP):
                    dve.wait_ge(xt_hi_done, t + 1)
                    dve.tensor_tensor(xt_lo[:, :, t * P:(t + 1) * P], ps[:, t, :].rearrange("p (k c) -> p k c", k=KT),
                                      xt_hi[:, :, t * P:(t + 1) * P].bitcast(F32), ALU.subtract).then_inc(xt_done, 1)

            def drain_v(unit, b):
                dve.wait_ge(proj_ready, unit * PROJ + (V_ + 1))
                dve.tensor_copy(v_t[:, :], bank(b, V_)).then_inc(proj_drained, 1)

            def lo_of_v(unit, b):
                dve.wait_ge(v_hi_done, unit + 1)
                dve.tensor_tensor(v_lo[:, b, :, :], bank(b, TURN).rearrange("p (t c) -> p t c", t=QB),
                                  v_hi[:, b, :, :].bitcast(F32), ALU.subtract).then_inc(proj_drained, 1)

            def cos_part(unit, b, i):
                dve.wait_ge(swapped, unit * 5 + (i + 1))
                wait(dve, rope_sum, unit * 5 + (i - 1))
                dve.tensor_tensor(direct[:, (5 * b + i) % 2, :], bank(b, i), cos[:, :],
                                  ALU.mult).then_inc(proj_drained, 1)

            def mask_and_max(n, j):
                cols = slice(0 if j else P, 2 * P)
                for h in range(GQ):
                    if h % 2 == 0:
                        dve.wait_ge(scores_ready, n * 2 + (h // 2 + 1))
                        dve.memset(waited[:, h // 2:h // 2 + 1], 0.0).then_inc(bank_seen, 1)
                    dve.tensor_tensor_reduce(probs[:, h, cols], ps_score[:, h, cols], mask[:, cols], -SM_SCALE, 3.0e38,
                                             ALU.add, ALU.min, neg_max[:, h:h + 1]).then_inc(shifted, 1)

            def normalise(n, j):
                cols = slice(0 if j else P, 2 * P)
                dve.wait_ge(exp_done, n * GQ + GQ)
                dve.reciprocal(inv[:, :], total[:, :]).then_inc(inv_done, 1)
                dve.wait_ge(inv_done, n + 1)
                for h in range(GQ):
                    dve.tensor_scalar(probs[:, h, cols], probs[:, h, cols], inv[:, h:h + 1], None,
                                      ALU.mult).then_inc(probs_ready, 1)

            def lo_of_probs(n, j):
                dve.wait_ge(pt_hi_done, n + 1)
                w = slice(0 if j else 1, 2)
                dve.tensor_tensor(pt_lo[:, w, :], ps_pt[:, w, :], pt_hi[:, w, :].bitcast(F32), ALU.subtract).then_inc(pt_split, 1)

            def lo_of_o(n, j):
                dve.wait_ge(o_hi_done, n + 1)
                dve.tensor_tensor(o_lo[:, j % 2, :, :], ps_o.rearrange("p (h c) -> p h c", h=GQ),
                                  o_hi[:, j % 2, :, :].bitcast(F32), ALU.subtract).then_inc(o_split, 1)

            def add_y(g, b, j):
                if isinstance(g, int) and (g, b, j) == (0, 0, 0):
                    return
                tile = (4 * b + j - 1) % TT
                if isinstance(g, int) and (g, b, j) == (0, 0, 1):
                    dve.wait_ge(y_zeroed, 1)
                dve.wait_ge(y_ready, g * 8 + (4 * b + j))
                if isinstance(g, int) and g == 0 and tile < TT - 1:
                    dve.tensor_copy(y[:, tile, :], ps_y).then_inc(y_added, 1)
                else:
                    dve.tensor_tensor(y[:, tile, :], ps_y, y[:, tile, :], ALU.add).then_inc(y_added, 1)

            def sum_rotation(i):
                dve.wait_ge(sin_part, i + 1)
                dve.wait_ge(proj_drained, i + 1)
                dve.tensor_tensor(roped[:, i % 2, :], roped[:, i % 2, :], direct[:, i % 2, :], ALU.add).then_inc(rope_sum, 1)

            statistics(range(0, GROUP))
            variance(0)
            normed(0)
            lo_of_x(0)
            statistics(range(GROUP, TT))
            variance(1)
            dve.wait_ge(table_in, 48)
            cos_part(0, 0, 0)
            sum_rotation(0)
            normed(1)
            cos_part(0, 0, 1)
            sum_rotation(1)
            cos_part(0, 0, 2)
            sum_rotation(2)
            lo_of_x(1)
            cos_part(0, 0, 3)
            sum_rotation(3)
            cos_part(0, 0, 4)
            drain_v(0, 0)
            sum_rotation(4)
            mask_and_max(0, 0)
            normalise(0, 0)
            lo_of_v(0, 0)

            def body(g, last):
                for b in range(2):
                    ahead = not (last and b == 1)
                    un, bn = (g * 2 + 1, 1) if b == 0 else (g * 2 + 2, 0)
                    for j in range(QB):
                        n = g * 8 + (4 * b + j)
                        nxt = g * 8 + (4 * b + j + 1)
                        if ahead and j == 0:
                            cos_part(un, bn, 0)
                        lo_of_probs(n, j)
                        if not ahead and j == QB - 1:
                            for at in FFN_AT[j]:
                                fw.dequantise(dve, 0, at)
                        if ahead and j == 3:
                            lo_of_v(un, bn)
                        if j == QB - 1:
                            add_y(g, b, j)
                        if j < QB - 1:
                            mask_and_max(nxt, j + 1)
                        elif ahead:
                            mask_and_max(nxt, 0)
                        if not ahead and j < QB - 1:
                            for at in FFN_AT[j]:
                                fw.dequantise(dve, 0, at)
                        if j < QB - 1:
                            normalise(nxt, j + 1)
                        elif ahead:
                            normalise(nxt, 0)
                        if ahead and j < QB - 1:
                            cos_part(un, bn, (1, 2, 4)[j])
                        if ahead and j == 2:
                            drain_v(un, bn)
                        if j < QB - 1:
                            add_y(g, b, j)
                        lo_of_o(n, j)
                        if ahead and j == 1:
                            cos_part(un, bn, 3)
            over_heads(dve, body)
            add_y(NKV - 1, 1, QB)


def build(nc, a, out):
    with ExitStack() as ctx:
        sh = Shared(nc, ctx)
        x = a["L0_attn_x"].rearrange("b s h -> (b s) h")
        fw = FfnWeights(sh, [a[f"L0_ffn_{m}_{v}"] for m in ("gate", "up", "down") for v in "wzs"])
        attention_block(nc, sh, fw, x, a["L0_attn_wq"], a["L0_attn_wk"], a["L0_attn_wv"], a["L0_attn_wo"],
                        a["rope_cos"], a["rope_sin"], a["mask"], a["ident"])
        ffn_block(nc, sh, fw, x, out.rearrange("b s h -> (b s) h"))


def shape_constants():
    half = P // 2
    inv_freq = (np.float32(10000.0) ** (-np.arange(half, dtype=np.float32) / np.float32(half))).astype(np.float32)
    angle = inv_freq[:, None] * np.arange(SEQ, dtype=np.float32)[None, :]
    cos, sin = np.cos(angle), np.sin(angle)
    q, c = np.arange(P)[:, None], np.arange(2 * P)[None, :]
    mask = np.where((c > q) & (c <= q + P), np.float32(0.0), np.float32(MASKED))
    return {
        "ident": np.eye(P, dtype=np.float32),
        "rope_cos": np.concatenate([cos, cos]),
        "rope_sin": np.concatenate([-sin, sin]),
        "mask": mask.astype(np.float32),
    }


def kernel(**inputs):
    import concourse.bacc as bacc
    from concourse.bass_utils import run_bass_kernel_spmd

    nc = bacc.Bacc("TRN2", target_bir_lowering=False, num_devices=1)
    arrays = {name: np.ascontiguousarray(a) for name, a in inputs.items()}
    arrays.update(shape_constants())
    aps = {name: nc.dram_tensor(name, a.shape, mybir.dt.from_np(a.dtype), kind="ExternalInput").ap()
           for name, a in arrays.items()}
    out = nc.dram_tensor("out", (BATCH, SEQ, HID), F32, kind="ExternalOutput").ap()
    build(nc, aps, out)
    r = run_bass_kernel_spmd(nc, [arrays], core_ids=[0])
    return r.results[0]["out"]
```
